# Optimizing a Trainium2 kernel written in Bass

```python
import numpy as np
import jax
import jax.numpy as jnp

def _softmax(x, axis=-1):
    return jax.nn.softmax(x, axis=axis)

def _gelu(x):
    return jax.nn.gelu(x, approximate=True)

def _silu(x):
    return jax.nn.silu(x)

def _sigmoid(x):
    return jax.nn.sigmoid(x)

def _layernorm(x, axis=-1, eps=1e-05):
    m = jnp.mean(x, axis=axis, keepdims=True)
    v = jnp.var(x, axis=axis, keepdims=True)
    return (x - m) / jnp.sqrt(v + eps)

def _scatter_add(tgt, idx, src, axis=0):
    return tgt.at[idx].add(src)

def _segment_sum(src, seg, n):
    return jax.ops.segment_sum(src, seg, n)
kernel_name = 'mk_xattn_ffn_d1_seqx_r8_947bfa'

def setup_inputs(seed: int=0):
    np.random.seed(seed)
    _w = jnp.asarray

    def _rec_inputs():
        import jax
        import jax.numpy as jnp
        _rk = jax.random.key(seed)
        x = -0.0005207 + 1.001 * jax.random.normal(jax.random.fold_in(_rk, 1), (16, 64, 128), jnp.float32)
        _lenS = 64 - jax.random.randint(jax.random.fold_in(_rk, 7), (16,), 0, max(1, 64 // 4) + 1, jnp.int32)
        _lenS2 = 64 - jax.random.randint(jax.random.fold_in(_rk, 8), (16,), 0, max(1, 64 // 4) + 1, jnp.int32)
        _ctx_512P = jax.random.normal(jax.random.fold_in(_rk, 11), (16, 16, 64), jnp.float32)
        _ctx_512c = jax.random.dirichlet(jax.random.fold_in(_rk, 511), 0.3 * jnp.ones((16,), jnp.float32), (16, 64))
        _ctx_512t = jnp.einsum('bsk,bkd->bsd', _ctx_512c, _ctx_512P)
        _ctx_512t = _ctx_512t * jax.lax.rsqrt(jnp.mean(jnp.square(_ctx_512t)) + 1e-12) * 0.953939
        ctx_512 = 0.502058 + 0.29099 * (_ctx_512t + 0.3 * jax.random.normal(jax.random.fold_in(_rk, 611), (16, 64, 64), jnp.float32))
        itok_BxS2xS_0_7 = jax.random.randint(jax.random.fold_in(_rk, 12), (16, 64, 64), 0, 8, jnp.int32)
        return (x, ctx_512, itok_BxS2xS_0_7)
    x, ctx_512, itok_BxS2xS_0_7 = _rec_inputs()

    def _L0_xattn_setup():
        import jax, jax.numpy as jnp
        import numpy as np
        key = jax.random.key(seed)
        k1, k2, k3, k4, k5 = jax.random.split(key, 5)
        B, K, S, E, I, D = (4, 2, 64, 8, 128, 256)
        x = jax.random.normal(k1, (B, S, I), dtype=jnp.float32)
        weights = jax.random.uniform(k2, (B, K, S), dtype=jnp.float32)
        ensembles = jax.random.randint(k3, (B, K, S), 0, E, dtype=jnp.int64)
        lim1 = float(np.sqrt(6.0 / (D + I)))
        proj_in = jax.random.uniform(k4, (E, D, I), dtype=jnp.float32, minval=-lim1, maxval=lim1)
        proj_out = jax.random.uniform(k5, (E, I, D), dtype=jnp.float32, minval=-lim1, maxval=lim1)
        return {'x': x, 'weights': weights, 'ensembles': ensembles, 'proj_in': proj_in, 'proj_out': proj_out}
    _L0_xattn_all = _L0_xattn_setup()
    _L0_xattn_in = {k: v for k, v in _L0_xattn_all.items() if k in ('proj_in', 'proj_out')}
    del _L0_xattn_all

    def _L0_ffn_setup():
        import jax, jax.numpy as jnp
        import numpy as np
        DIM = 128
        HIDDEN = 384
        SCALE = 1.0 / 127.0

        def _dequant(w_int, dtype):
            return w_int.astype(dtype) * jnp.asarray(SCALE, dtype)
        key = jax.random.key(seed)
        k_x, k_g, k_u, k_d = jax.random.split(key, 4)
        x = jax.random.normal(k_x, (4, 256, DIM), dtype=jnp.float32)
        w_gate = jax.random.randint(k_g, (HIDDEN, DIM), -127, 128, dtype=jnp.int32)
        w_up = jax.random.randint(k_u, (HIDDEN, DIM), -127, 128, dtype=jnp.int32)
        w_down = jax.random.randint(k_d, (DIM, HIDDEN), -127, 128, dtype=jnp.int32)
        return {'x': x, 'w_gate': w_gate, 'w_up': w_up, 'w_down': w_down}
    _L0_ffn_all = _L0_ffn_setup()
    _L0_ffn_in = {k: v for k, v in _L0_ffn_all.items() if k in ('w_gate', 'w_up', 'w_down')}
    del _L0_ffn_all
    return {'x': x, 'ctx_512': ctx_512, 'itok_BxS2xS_0_7': itok_BxS2xS_0_7, 'L0_xattn_proj_in': _L0_xattn_in['proj_in'], 'L0_xattn_proj_out': _L0_xattn_in['proj_out'], 'L0_ffn_w_gate': _L0_ffn_in['w_gate'], 'L0_ffn_w_up': _L0_ffn_in['w_up'], 'L0_ffn_w_down': _L0_ffn_in['w_down']}

def reference(x, ctx_512, itok_BxS2xS_0_7, L0_xattn_proj_in, L0_xattn_proj_out, L0_ffn_w_gate, L0_ffn_w_up, L0_ffn_w_down):
    import jax
    import jax.numpy as jnp

    def _L0_xattn_ref(x, weights, ensembles, proj_in, proj_out):
        import jax, jax.numpy as jnp
        import numpy as np
        E = proj_in.shape[0]
        h = jax.nn.relu(jnp.einsum('edi,bsi->bsed', proj_in, x))
        o = jnp.einsum('eid,bsed->bsei', proj_out, h)
        onehot = jax.nn.one_hot(ensembles, E, dtype=x.dtype)
        gate = jnp.einsum('bks,bkse->bse', weights, onehot)
        return jnp.einsum('bsei,bse->bsi', o, gate)

    def _L0_ffn_ref(x, w_gate, w_up, w_down):
        import jax, jax.numpy as jnp
        import numpy as np
        DIM = 128
        HIDDEN = 384
        SCALE = 1.0 / 127.0

        def _dequant(w_int, dtype):
            return w_int.astype(dtype) * jnp.asarray(SCALE, dtype)
        wg = _dequant(w_gate, x.dtype)
        wu = _dequant(w_up, x.dtype)
        wd = _dequant(w_down, x.dtype)
        gate = jnp.einsum('bsd,hd->bsh', x, wg)
        up = jnp.einsum('bsd,hd->bsh', x, wu)
        h = jax.nn.silu(gate) * up
        return jnp.einsum('bsh,dh->bsd', h, wd)
    x = x + _L0_xattn_ref(_layernorm(x, axis=-1), ctx_512, itok_BxS2xS_0_7, L0_xattn_proj_in, L0_xattn_proj_out)
    x = x + _L0_ffn_ref(_layernorm(x, axis=-1), L0_ffn_w_gate, L0_ffn_w_up, L0_ffn_w_down)
    return x

_drawn_inputs = setup_inputs


def setup_inputs(seed=0):
    import zlib

    import numpy as np

    out = dict(_drawn_inputs(seed))
    spreads = {}
    factors = {}
    for name, (base, spread) in spreads.items():
        noise = np.random.default_rng([zlib.crc32(name.encode()), seed]).standard_normal(out[name].shape)
        drawn = base * np.exp(spread * noise) if base else spread * noise
        out[name] = jnp.asarray(drawn.astype(out[name].dtype))
    for name, factor in factors.items():
        out[name] = (out[name] * factor).astype(out[name].dtype)
    return out
```

```python
import concourse.bass as bass
from concourse import mybir
from contextlib import ExitStack


def xattn_ffn_program(
    nc: bass.Bass,
    x_tok: bass.AP,
    x_feat: bass.AP,
    ctx_kt: bass.AP,
    ids_kt: bass.AP,
    w_experts: bass.AP,
    w_ffn: bass.AP,
    out_feat: bass.AP,
):
    f32 = mybir.dt.float32
    f32r = mybir.dt.float32r
    i32 = mybir.dt.int32
    ALU = mybir.AluOpType
    ACT = mybir.ActivationFunctionType

    P = 128
    E = w_experts.shape[1]
    T = x_feat.shape[1]
    N = 512
    HALVES = T // N
    TPH = N // P
    STEPS = HALVES * E
    CH = w_experts.shape[2] // 2 // P
    M = STEPS * CH
    FC = w_ffn.shape[1] // 3 // P
    J = HALVES * FC
    LAG = 2
    EPS = 1e-5
    SCALE = 1.0 / 127.0

    with ExitStack() as ctx:
        def sb(name, shape, dt=f32):
            return ctx.enter_context(nc.sbuf_tensor(name, shape, dt))

        def bank(name):
            return ctx.enter_context(nc.psum_tensor(name, [P, N], f32))

        def sem(name):
            return ctx.enter_context(nc.semaphore(name))

        xt = sb("xt", [P, T // P, P])
        acc = sb("acc", [P, T])
        cw = sb("cw", [P, T])
        ids = sb("ids", [P, T], i32)
        we = sb("we", [P, E, 2 * CH * P])
        wf = sb("wf", [P, 3 * FC * P], i32)
        ident = sb("ident", [P, P])
        ones = sb("ones", [P, P], f32r)
        neg_half = sb("neg_half", [P, TPH])
        warm = sb("warm", [P, 1])
        stats = sb("stats", [P, 2 * HALVES, TPH, 6])
        mv = sb("mv", [P, 2 * HALVES, TPH, 2])
        veps = sb("veps", [P, 2 * HALVES, TPH])
        rstd = sb("rstd", [P, 2 * HALVES, TPH])
        xn = sb("xn", [P, 2, TPH, P])
        nh = sb("nh", [P, 2 * HALVES, N], f32r)
        nl = sb("nl", [P, 2 * HALVES, N], f32r)
        weh = sb("weh", [P, E, 2 * CH * P], f32r)
        wel = sb("wel", [P, E, 2 * CH * P], f32r)
        wff = sb("wff", [P, 3 * FC * P])
        wfh = sb("wfh", [P, 3 * FC * P], f32r)
        wfl = sb("wfl", [P, 3 * FC * P], f32r)
        chl = sb("chl", [P, T], f32r)
        MR = 3
        msk = sb("msk", [P, MR, N], f32r)
        gbc = sb("gbc", [P, 2, N])
        gated = sb("gated", [P, 2, N])
        HR = 4
        hh = sb("hh", [P, HR, N], f32r)
        hl = sb("hl", [P, HR, N], f32r)
        sg = sb("sg", [P, 2, N])
        prod = sb("prod", [P, 2, N])
        fh = sb("fh", [P, J, N], f32r)
        fl = sb("fl", [P, J, N], f32r)
        res = sb("res", [P, T])

        hid = [bank(f"hid{i}") for i in range(HR)]
        outp = [bank(f"outp{i}") for i in range(2)]
        gate_ps = bank("gate_ps")
        tr_ps = bank("tr_ps")

        x_in = [sem(f"x_in{h}") for h in range(HALVES)]
        cw_in = [sem(f"cw_in{h}") for h in range(HALVES)]
        ids_in = [sem(f"ids_in{h}") for h in range(HALVES)]
        we_in = [sem(f"we_in{e}") for e in range(E)]
        wf_in = sem("wf_in")
        acc_in = sem("acc_in")
        zeroed = sem("zeroed")
        ident_ready = sem("ident_ready")
        consts_ready = sem("consts_ready")
        stats_ready = sem("stats_ready")
        aggr_ready = sem("aggr_ready")
        veps_ready = sem("veps_ready")
        rstd_ready = sem("rstd_ready")
        norm_ready = sem("norm_ready")
        y_turned = sem("y_turned")
        n_turned = sem("n_turned")
        nh_ready = sem("nh_ready")
        nl_ready = sem("nl_ready")
        w_hi = sem("w_hi")
        w_float = sem("w_float")
        w_lo = sem("w_lo")
        w0_lo = sem("w0_lo")
        chi_ready = sem("chi_ready")
        chl_ready = sem("chl_ready")
        mask_ready = sem("mask_ready")
        gate_done = sem("gate_done")
        gbc_ready = sem("gbc_ready")
        hid_done = sem("hid_done")
        hh_ready = sem("hh_ready")
        hl_ready = sem("hl_ready")
        out_done = sem("out_done")
        gated_ready = sem("gated_ready")
        acc_done = sem("acc_done")
        up_done = sem("up_done")
        sg_ready = sem("sg_ready")
        prod_ready = sem("prod_ready")
        fh_ready = sem("fh_ready")
        fl_ready = sem("fl_ready")
        down_done = sem("down_done")
        res_ready = sem("res_ready")
        stored = sem("stored")

        block = ctx.enter_context(nc.Block())

        def half(t, h):
            return t[:, h * N:(h + 1) * N]

        @block.sync
        def _(sp):
            def load_routing(h):
                sp.dma_start(half(cw, h), half(ctx_kt, h)).then_inc(cw_in[h], 16)
                sp.dma_start(half(ids, h), half(ids_kt, h)).then_inc(ids_in[h], 16)

            def load_expert(e):
                sp.dma_start(we[:, e, :], w_experts[:, e, :]).then_inc(we_in[e], 16)

            def load_x(h):
                sp.dma_start(xt[:, h * TPH:(h + 1) * TPH, :],
                             x_tok[:, h * TPH:(h + 1) * TPH, :]).then_inc(x_in[h], 16)

            load_x(0)
            load_expert(0)
            load_routing(0)
            load_expert(1)
            load_x(1)
            load_expert(2)
            sp.dma_start(acc[:, :], x_feat).then_inc(acc_in, 16)
            for e in range(3, E):
                load_expert(e)
            load_routing(1)
            sp.dma_start(wf[:, :], w_ffn).then_inc(wf_in, 16)
            for h in range(HALVES):
                sp.wait_ge(res_ready, h + 1)
                sp.dma_start(half(out_feat, h), half(res, h)).then_inc(stored, 16)
            sp.wait_ge(stored, 16 * HALVES)

        @block.gpsimd
        def _(pool):
            def lo_expert(e):
                pool.wait_ge(w_hi, e + 1)
                nc.gpsimd.tensor_tensor(wel[:, e, :], we[:, e, :], weh[:, e, :].bitcast(f32),
                                        ALU.subtract).then_inc(w_lo, 1)

            def lo_ffn(b):
                pool.wait_ge(w_float, b + 1)
                pool.wait_ge(w_hi, E + b + 1)
                c = slice(b * FC * P, (b + 1) * FC * P)
                nc.gpsimd.tensor_tensor(wfl[:, c], wff[:, c], wfh[:, c].bitcast(f32),
                                        ALU.subtract).then_inc(w_lo, 1)

            def reciprocal_root(g):
                pool.wait_ge(veps_ready, g + 1)
                nc.gpsimd.tensor_tensor(rstd[:, g, :], veps[:, g, :], neg_half[:, :],
                                        ALU.pow).then_inc(rstd_ready, 1)

            def accumulate(n):
                h = n // E
                if n == 0:
                    pool.wait_ge(acc_in, 16)
                else:
                    pool.wait_ge(acc_done, n)
                pool.wait_ge(gated_ready, n + 1)
                nc.gpsimd.tensor_tensor(half(acc, h), half(acc, h), gated[:, n % 2, :],
                                        ALU.add).then_inc(acc_done, 1)

            nc.gpsimd.memset(ident[:, :], 0.0).then_inc(zeroed, 1)
            nc.gpsimd.memset(neg_half[:, :], -0.5).then_inc(zeroed, 1)
            nc.gpsimd.memset(ones[:, :].bitcast(f32), 1.0).then_inc(consts_ready, 1)
            pool.wait_ge(zeroed, 2)
            nc.gpsimd.affine_select(out=ident[:, :], in_=ident[:, :], compare_op=ALU.not_equal, fill=1.0,
                                    base=0, pattern=[[-1, P]], channel_multiplier=1).then_inc(ident_ready, 1)
            reciprocal_root(0)
            lo_expert(1)
            reciprocal_root(1)
            lo_expert(2)
            for n in range(STEPS):
                if 3 <= n + 3 < E:
                    lo_expert(n + 3)
                if E <= n < E + 3:
                    lo_ffn(n - E)
                accumulate(n)
                if n == E + 1:
                    reciprocal_root(HALVES)
            reciprocal_root(HALVES + 1)

        @block.scalar
        def _(act):
            def hi_expert(e):
                act.wait_ge(we_in[e], 16)
                nc.scalar.activation(weh[:, e, :], we[:, e, :], ACT.Copy).then_inc(w_hi, 1)

            def hi_ffn(b):
                if b == 0:
                    act.wait_ge(wf_in, 16)
                c = slice(b * FC * P, (b + 1) * FC * P)
                nc.scalar.activation(wff[:, c], wf[:, c], ACT.Copy).then_inc(w_float, 1)
                nc.scalar.activation(wfh[:, c], wf[:, c], ACT.Copy).then_inc(w_hi, 1)

            def hi_norm(g):
                act.wait_ge(n_turned, g + 1)
                nc.scalar.activation(nh[:, g, :], tr_ps[:, :], ACT.Copy).then_inc(nh_ready, 1)

            def gate_copy(n):
                act.wait_ge(gate_done, n + 1)
                if n >= 2:
                    act.wait_ge(gated_ready, n - 1)
                nc.scalar.activation(gbc[:, n % 2, :], gate_ps[:, :], ACT.Copy).then_inc(gbc_ready, 1)

            def hi_hidden(m):
                act.wait_ge(hid_done, m + 1)
                if m >= HR:
                    act.wait_ge(out_done, m - HR + 1)
                nc.scalar.activation(hh[:, m % HR, :], hid[m % HR][:, :], ACT.Relu).then_inc(hh_ready, 1)

            def silu(j):
                act.wait_ge(up_done, j + 1)
                if j >= 2:
                    act.wait_ge(prod_ready, j - 1)
                nc.scalar.activation(sg[:, j % 2, :], hid[2 * j % HR][:, :], ACT.Silu,
                                     scale=SCALE).then_inc(sg_ready, 1)

            def hi_prod(j):
                act.wait_ge(prod_ready, j + 1)
                nc.scalar.activation(fh[:, j, :], prod[:, j % 2, :], ACT.Copy).then_inc(fh_ready, 1)

            act.wait_ge(consts_ready, 1)
            nc.scalar.activation(warm[:, :], ones[:, 0:1].bitcast(f32), ACT.Silu)
            hi_expert(0)
            hi_norm(0)
            hi_expert(1)
            hi_expert(2)
            for m in range(M):
                if m == 5:
                    hi_norm(1)
                if m == 24:
                    hi_norm(2)
                hi_hidden(m)
                if m % 2 == 0:
                    gate_copy(m // 2)
                else:
                    if m // 2 + 3 < E:
                        hi_expert(m // 2 + 3)
                    if E <= m // 2 + 1 < E + 3:
                        hi_ffn(m // 2 + 1 - E)
            for j in range(FC):
                silu(j)
                hi_prod(j)
            hi_norm(3)
            for j in range(FC, J):
                silu(j)
                hi_prod(j)

        @block.vector
        def _(dve):
            def layernorm_stats(g):
                if g < HALVES:
                    dve.wait_ge(x_in[g], 16)
                else:
                    dve.wait_ge(y_turned, g - HALVES + 1)
                for j in range(TPH):
                    src = xt[:, g * TPH + j, :] if g < HALVES else tr_ps[:, j * P:(j + 1) * P]
                    nc.vector.bn_stats(stats[:, g, j, :], src).then_inc(stats_ready, 1)
                for j in range(TPH):
                    dve.wait_ge(stats_ready, g * TPH + j + 1)
                    nc.vector.bn_aggr(mv[:, g, j, :], stats[:, g, j, :]).then_inc(aggr_ready, 1)
                dve.wait_ge(aggr_ready, (g + 1) * TPH)
                nc.vector.tensor_scalar(veps[:, g, :], mv[:, g, :, 1], EPS, None, ALU.add).then_inc(veps_ready, 1)

            def normalise(g):
                dve.wait_ge(rstd_ready, g + 1)
                if g >= 2:
                    dve.wait_ge(n_turned, g - 1)
                for j in range(TPH):
                    src = xt[:, g * TPH + j, :] if g < HALVES else tr_ps[:, j * P:(j + 1) * P]
                    nc.vector.tensor_scalar(xn[:, g % 2, j, :], src, mv[:, g, j, 0:1], rstd[:, g, j:j + 1],
                                            ALU.subtract, ALU.mult).then_inc(norm_ready, 1)

            def lo_norm(g):
                dve.wait_ge(nh_ready, g + 1)
                nc.vector.tensor_tensor(nl[:, g, :], tr_ps[:, :], nh[:, g, :].bitcast(f32),
                                        ALU.subtract).then_inc(nl_ready, 1)

            def lo_expert_0():
                dve.wait_ge(w_hi, 1)
                nc.vector.tensor_tensor(wel[:, 0, :], we[:, 0, :], weh[:, 0, :].bitcast(f32),
                                        ALU.subtract).then_inc(w0_lo, 1)

            def split_routing(h):
                dve.wait_ge(cw_in[h], 16)
                nc.vector.tensor_copy(half(chl, h), half(cw, h)).then_inc(chi_ready, 1)
                dve.wait_ge(chi_ready, h + 1)
                low = chl[P // 2:P, h * N:(h + 1) * N]
                nc.vector.tensor_tensor(low, cw[P // 2:P, h * N:(h + 1) * N], low.bitcast(f32),
                                        ALU.subtract).then_inc(chl_ready, 1)

            def mask(n):
                h = n // E
                if n % E == 0:
                    dve.wait_ge(ids_in[h], 16)
                    dve.wait_ge(chl_ready, h + 1)
                if n >= MR:
                    dve.wait_ge(gate_done, n - MR + 1)
                nc.vector.scalar_tensor_tensor(out=msk[:, n % MR, :], in0=half(ids, h), scalar=float(n % E),
                                               in1=half(chl, h).bitcast(f32),
                                               op0=ALU.is_equal, op1=ALU.mult).then_inc(mask_ready, 1)

            def lo_hidden(m):
                dve.wait_ge(hh_ready, m + 1)
                nc.vector.scalar_tensor_tensor(out=hl[:, m % HR, :], in0=hid[m % HR][:, :], scalar=0.0,
                                               in1=hh[:, m % HR, :].bitcast(f32),
                                               op0=ALU.max, op1=ALU.subtract).then_inc(hl_ready, 1)

            def apply_gate(n):
                dve.wait_ge(out_done, 2 * n + 2)
                dve.wait_ge(gbc_ready, n + 1)
                if n >= 2:
                    dve.wait_ge(acc_done, n - 1)
                nc.vector.tensor_tensor(gated[:, n % 2, :], outp[n % 2][:, :], gbc[:, n % 2, :],
                                        ALU.mult).then_inc(gated_ready, 1)

            def multiply(j):
                dve.wait_ge(sg_ready, j + 1)
                if j >= 2:
                    dve.wait_ge(fh_ready, j - 1)
                nc.vector.tensor_tensor(prod[:, j % 2, :], hid[(2 * j + 1) % HR][:, :], sg[:, j % 2, :],
                                        ALU.mult).then_inc(prod_ready, 1)

            def lo_prod(j):
                dve.wait_ge(fh_ready, j + 1)
                nc.vector.tensor_tensor(fl[:, j, :], prod[:, j % 2, :], fh[:, j, :].bitcast(f32),
                                        ALU.subtract).then_inc(fl_ready, 1)

            def finish(h):
                dve.wait_ge(down_done, h + 1)
                nc.vector.scalar_tensor_tensor(out=half(res, h), in0=outp[h][:, :], scalar=SCALE * SCALE,
                                               in1=half(acc, h), op0=ALU.mult, op1=ALU.add).then_inc(res_ready, 1)

            layernorm_stats(0)
            split_routing(0)
            lo_expert_0()
            normalise(0)
            mask(0)
            lo_norm(0)
            mask(1)
            layernorm_stats(1)
            for m in range(M):
                if m == 3:
                    normalise(1)
                if m == 6:
                    lo_norm(1)
                if m == 11:
                    split_routing(1)
                if m == 20:
                    layernorm_stats(2)
                if m == 23:
                    normalise(2)
                if m == 25:
                    lo_norm(2)
                lo_hidden(m)
                if m % 2 == 0:
                    if m // 2 + 2 < STEPS:
                        mask(m // 2 + 2)
                elif m >= 3:
                    apply_gate((m - 3) // 2)
            apply_gate(STEPS - 1)
            multiply(0)
            lo_prod(0)
            layernorm_stats(3)
            multiply(1)
            lo_prod(1)
            normalise(3)
            multiply(2)
            lo_prod(2)
            lo_norm(3)
            finish(0)
            for j in range(FC, J):
                multiply(j)
                lo_prod(j)
            finish(1)

        @block.tensor
        def _(pe):
            def turn_norm(g):
                if g == 0:
                    pe.wait_ge(ident_ready, 1)
                else:
                    pe.wait_ge(nl_ready, g)
                pe.wait_ge(norm_ready, TPH * (g + 1))
                for j in range(TPH):
                    last = nc.tensor.transpose(tr_ps[:, j * P:(j + 1) * P], xn[:, g % 2, j, :], ident[:, :])
                last.then_inc(n_turned, 1)

            def turn_y(h):
                pe.wait_ge(nl_ready, HALVES + h)
                pe.wait_ge(acc_done, E * (h + 1))
                for j in range(TPH):
                    c = h * N + j * P
                    last = nc.tensor.transpose(tr_ps[:, j * P:(j + 1) * P], acc[:, c:c + P], ident[:, :])
                last.then_inc(y_turned, 1)

            def gate(n):
                if n == 0:
                    pe.wait_ge(consts_ready, 1)
                else:
                    pe.wait_ge(gbc_ready, n)
                pe.wait_ge(mask_ready, n + 1)
                nc.tensor.matmul(gate_ps[:, :], ones[:, :], msk[:, n % MR, :],
                                 start=True, stop=True).then_inc(gate_done, 1)

            def three(dst, wh, wl, xh, xl, start=True, stop=True):
                nc.tensor.matmul(dst, wh, xh, start=start, stop=False)
                nc.tensor.matmul(dst, wl, xh, start=False, stop=False)
                return nc.tensor.matmul(dst, wh, xl, start=False, stop=stop)

            def first_product(m):
                n, c = m // CH, m % CH
                h, e = n // E, n % E
                if c == 0 and h == 0:
                    if e == 0:
                        pe.wait_ge(w0_lo, 1)
                    else:
                        pe.wait_ge(w_lo, e)
                if m % (M // HALVES) == 0:
                    pe.wait_ge(nl_ready, h + 1)
                if m >= HR:
                    pe.wait_ge(hl_ready, m - HR + 1)
                w = slice(c * P, (c + 1) * P)
                three(hid[m % HR][:, :], weh[:, e, w], wel[:, e, w],
                      nh[:, h, :], nl[:, h, :]).then_inc(hid_done, 1)

            def second_product(m):
                n, c = m // CH, m % CH
                e = n % E
                if c == 0 and n >= 2:
                    pe.wait_ge(gated_ready, n - 1)
                pe.wait_ge(hl_ready, m + 1)
                w = slice((CH + c) * P, (CH + c + 1) * P)
                three(outp[n % 2][:, :], weh[:, e, w], wel[:, e, w],
                      hh[:, m % HR, :], hl[:, m % HR, :],
                      start=(c == 0), stop=(c == CH - 1)).then_inc(out_done, 1)

            def gate_up(j):
                h, c = j // FC, j % FC
                if j < 2:
                    pe.wait_ge(hl_ready, M - 2 + 2 * j)
                else:
                    pe.wait_ge(prod_ready, j - 1)
                if c == 0:
                    pe.wait_ge(nl_ready, HALVES + h + 1)
                if j == 0:
                    pe.wait_ge(w_lo, E + 2)
                g = HALVES + h
                for b in range(2):
                    w = slice((b * FC + c) * P, (b * FC + c + 1) * P)
                    last = three(hid[(2 * j + b) % HR][:, :], wfh[:, w], wfl[:, w], nh[:, g, :], nl[:, g, :])
                last.then_inc(up_done, 1)

            def down(h):
                pe.wait_ge(gated_ready, STEPS - 1 + h)
                for c in range(FC):
                    j = h * FC + c
                    pe.wait_ge(fl_ready, j + 1)
                    w = slice((2 * FC + c) * P, (2 * FC + c + 1) * P)
                    last = three(outp[h][:, :], wfh[:, w], wfl[:, w], fh[:, j, :], fl[:, j, :],
                                 start=(c == 0), stop=(c == FC - 1))
                last.then_inc(down_done, 1)

            turn_norm(0)
            for m in range(M + LAG):
                if m == 4:
                    turn_norm(1)
                if m == 20:
                    turn_y(0)
                if m == 24:
                    turn_norm(2)
                if m < M:
                    if m % CH == 0:
                        gate(m // CH)
                    first_product(m)
                if m >= LAG:
                    second_product(m - LAG)
            gate_up(0)
            turn_y(1)
            gate_up(1)
            gate_up(2)
            turn_norm(3)
            down(0)
            for j in range(FC, J):
                gate_up(j)
            down(1)


def kernel(x, ctx_512, itok_BxS2xS_0_7, L0_xattn_proj_in, L0_xattn_proj_out,
           L0_ffn_w_gate, L0_ffn_w_up, L0_ffn_w_down):
    import numpy as np
    import concourse.bacc as bacc
    from concourse import mybir
    from concourse.bass_utils import run_bass_kernel_spmd

    P = 128
    x = np.asarray(x)
    B, S, D = x.shape
    T = B * S
    win, wout = np.asarray(L0_xattn_proj_in), np.asarray(L0_xattn_proj_out)
    E, HID, _ = win.shape
    CH = HID // P
    rows = x.reshape(T, D)
    w_experts = np.concatenate(
        [win.transpose(2, 0, 1), wout.reshape(E, D, CH, P).transpose(3, 0, 2, 1).reshape(P, E, CH * D)], axis=2)
    down = np.asarray(L0_ffn_w_down).T
    w_ffn = np.concatenate(
        [np.asarray(L0_ffn_w_gate).T, np.asarray(L0_ffn_w_up).T,
         down.reshape(-1, P, D).transpose(1, 0, 2).reshape(P, -1)], axis=1)
    def choices_first(a):
        a = np.asarray(a).transpose(1, 0, 2).reshape(-1, T)
        return np.concatenate([a, a], axis=0)

    arrays = {
        "x_tok": rows.reshape(T // P, P, D).transpose(1, 0, 2),
        "x_feat": rows.T,
        "ctx_kt": choices_first(ctx_512),
        "ids_kt": choices_first(itok_BxS2xS_0_7),
        "w_experts": w_experts,
        "w_ffn": w_ffn,
    }
    arrays = {k: np.ascontiguousarray(v) for k, v in arrays.items()}
    nc = bacc.Bacc("TRN2", target_bir_lowering=False, num_devices=1)
    ins = [nc.dram_tensor(k, v.shape, mybir.dt.from_np(v.dtype), kind="ExternalInput").ap()
           for k, v in arrays.items()]
    out = nc.dram_tensor("out_feat", (D, T), mybir.dt.float32, kind="ExternalOutput").ap()
    xattn_ffn_program(nc, *ins, out)
    r = run_bass_kernel_spmd(nc, [arrays], core_ids=[0])
    return np.ascontiguousarray(r.results[0]["out_feat"].T).reshape(B, S, D)
```

```python
import concourse.bass as bass
from concourse import mybir
from contextlib import ExitStack


def xattn_ffn_program(
    nc: bass.Bass,
    x_tok: bass.AP,
    x_feat: bass.AP,
    ctx_kt: bass.AP,
    ids_kt: bass.AP,
    w_experts: bass.AP,
    w_ffn: bass.AP,
    out_feat: bass.AP,
):
    f32 = mybir.dt.float32
    f32r = mybir.dt.float32r
    i32 = mybir.dt.int32
    ALU = mybir.AluOpType
    ACT = mybir.ActivationFunctionType

    P = 128
    E = w_experts.shape[1]
    T = x_feat.shape[1]
    N = 512
    HALVES = T // N
    TPH = N // P
    STEPS = HALVES * E
    CH = w_experts.shape[2] // 2 // P
    M = STEPS * CH
    FC = w_ffn.shape[1] // 3 // P
    J = HALVES * FC
    LAG = 2
    SHARED = [0, 2 * HALVES - 1]
    BY_POOL = 2
    WARM = 16
    EPS = 1e-5
    SCALE = 1.0 / 127.0

    with ExitStack() as ctx:
        def sb(name, shape, dt=f32):
            return ctx.enter_context(nc.sbuf_tensor(name, shape, dt))

        def bank(name):
            return ctx.enter_context(nc.psum_tensor(name, [P, N], f32))

        def sem(name):
            return ctx.enter_context(nc.semaphore(name))

        xt = sb("xt", [P, T // P, P])
        acc = sb("acc", [P, T])
        cw = sb("cw", [P, T])
        ids = sb("ids", [P, T], i32)
        we = sb("we", [P, E, 2 * CH * P])
        wf = sb("wf", [P, 3 * FC * P], i32)
        ident = sb("ident", [P, P])
        ones = sb("ones", [P, P], f32r)
        neg_half = sb("neg_half", [P, TPH])
        warm = sb("warm", [P, 1])
        zero = sb("zero", [P, N], f32r)
        stats = sb("stats", [P, 2 * HALVES, TPH, 6])
        mv = sb("mv", [P, 2 * HALVES, TPH, 2])
        veps = sb("veps", [P, 2 * HALVES, TPH])
        rstd = sb("rstd", [P, 2 * HALVES, TPH])
        shift = sb("shift", [P, 2 * HALVES, TPH // 2])
        xn = sb("xn", [P, 2, TPH, P])
        nh = sb("nh", [P, 2 * HALVES, N], f32r)
        nl = sb("nl", [P, 2 * HALVES, N], f32r)
        weh = sb("weh", [P, E, 2 * CH * P], f32r)
        wel = sb("wel", [P, E, 2 * CH * P], f32r)
        wff = sb("wff", [P, 3 * FC * P])
        wfh = sb("wfh", [P, 3 * FC * P], f32r)
        wfl = sb("wfl", [P, 3 * FC * P], f32r)
        chl = sb("chl", [P, T], f32r)
        MR = 3
        msk = sb("msk", [P, MR, N], f32r)
        gbc = sb("gbc", [P, 2, N])
        gated = sb("gated", [P, 2, N])
        HR = 4
        hh = sb("hh", [P, HR, N], f32r)
        hl = sb("hl", [P, HR, N], f32r)
        sg = sb("sg", [P, 2, N])
        prod = sb("prod", [P, 2, N])
        fh = sb("fh", [P, J, N], f32r)
        fl = sb("fl", [P, J, N], f32r)
        res = sb("res", [P, T])

        hid = [bank(f"hid{i}") for i in range(HR)]
        outp = [bank(f"outp{i}") for i in range(2)]
        gate_ps = bank("gate_ps")
        tr_ps = bank("tr_ps")

        x0_in = [sem(f"x0_in{i}") for i in range(2)]
        x1_in = sem("x1_in")
        cw_in = [sem(f"cw_in{h}") for h in range(HALVES)]
        ids_in = [sem(f"ids_in{h}") for h in range(HALVES)]
        we_in = [sem(f"we_in{e}") for e in range(E)]
        wf_in = sem("wf_in")
        acc_in = sem("acc_in")
        zeroed = sem("zeroed")
        ident_ready = sem("ident_ready")
        consts_ready = sem("consts_ready")
        stats_ready = sem("stats_ready")
        aggr_ready = sem("aggr_ready")
        veps_ready = sem("veps_ready")
        rstd_ready = sem("rstd_ready")
        norm_ready = sem("norm_ready")
        y_turned = sem("y_turned")
        shift_ready = sem("shift_ready")
        norm_act_ready = sem("norm_act_ready")
        n_turned = sem("n_turned")
        nh_ready = sem("nh_ready")
        nl_ready = sem("nl_ready")
        w_hi = sem("w_hi")
        w_float = sem("w_float")
        w_lo = sem("w_lo")
        acc_last = sem("acc_last")
        zero_ready = sem("zero_ready")
        chi_ready = sem("chi_ready")
        chl_ready = sem("chl_ready")
        mask_ready = sem("mask_ready")
        gate_done = sem("gate_done")
        gbc_ready = sem("gbc_ready")
        hid_done = sem("hid_done")
        hh_ready = sem("hh_ready")
        hl_ready = sem("hl_ready")
        out_done = sem("out_done")
        gated_ready = sem("gated_ready")
        acc_done = sem("acc_done")
        up_done = sem("up_done")
        sg_ready = sem("sg_ready")
        prod_ready = sem("prod_ready")
        fh_ready = sem("fh_ready")
        fl_pool_ready = sem("fl_pool_ready")
        fl_ready = sem("fl_ready")
        down_done = sem("down_done")
        res_ready = sem("res_ready")
        stored = sem("stored")

        block = ctx.enter_context(nc.Block())

        def turned_tile(h, j):
            if h == HALVES - 1 and j >= TPH // 2:
                return gate_ps[:, (j - TPH // 2) * P:(j - TPH // 2 + 1) * P]
            return tr_ps[:, j * P:(j + 1) * P]

        def half(t, h):
            return t[:, h * N:(h + 1) * N]

        @block.sync
        def _(sp):
            def load_routing(h):
                sp.dma_start(half(cw, h), half(ctx_kt, h)).then_inc(cw_in[h], 16)
                sp.dma_start(half(ids, h), half(ids_kt, h)).then_inc(ids_in[h], 16)

            def load_expert(e):
                sp.dma_start(we[:, e, :], w_experts[:, e, :]).then_inc(we_in[e], 16)

            for t in range(0, TPH, 2):
                sp.dma_start(xt[:, t:t + 2, :], x_tok[:, t:t + 2, :]).then_inc(x0_in[t // 2], 16)
            load_expert(0)
            load_routing(0)
            load_expert(1)
            sp.dma_start(xt[:, TPH:2 * TPH, :], x_tok[:, TPH:2 * TPH, :]).then_inc(x1_in, 16)
            load_expert(2)
            sp.dma_start(acc[:, :], x_feat).then_inc(acc_in, 16)
            for e in range(3, E):
                load_expert(e)
            load_routing(1)
            sp.dma_start(wf[:, :], w_ffn).then_inc(wf_in, 16)
            for h in range(HALVES):
                sp.wait_ge(res_ready, h + 1)
                sp.dma_start(half(out_feat, h), half(res, h)).then_inc(stored, 16)
            sp.wait_ge(stored, 16 * HALVES)

        @block.gpsimd
        def _(pool):
            def lo_expert(e):
                pool.wait_ge(w_hi, e + 1)
                nc.gpsimd.tensor_tensor(wel[:, e, :], we[:, e, :], weh[:, e, :].bitcast(f32),
                                        ALU.subtract).then_inc(w_lo, 1)

            def lo_ffn(b):
                pool.wait_ge(w_float, b + 1)
                pool.wait_ge(w_hi, E + b + 1)
                c = slice(b * FC * P, (b + 1) * FC * P)
                nc.gpsimd.tensor_tensor(wfl[:, c], wff[:, c], wfh[:, c].bitcast(f32),
                                        ALU.subtract).then_inc(w_lo, 1)

            def reciprocal_root(g):
                pool.wait_ge(veps_ready, g + 1)
                nc.gpsimd.tensor_tensor(rstd[:, g, :], veps[:, g, :], neg_half[:, :],
                                        ALU.pow).then_inc(rstd_ready, 1)

            def lo_prod(j):
                pool.wait_ge(fh_ready, j + 1)
                nc.gpsimd.tensor_tensor(fl[:, j, :], prod[:, j % 2, :], fh[:, j, :].bitcast(f32),
                                        ALU.subtract).then_inc(fl_pool_ready, 1)

            def accumulate(n):
                h = n // E
                if n == 0:
                    pool.wait_ge(acc_in, 16)
                else:
                    pool.wait_ge(acc_done, n)
                pool.wait_ge(gated_ready, n + 1)
                nc.gpsimd.tensor_tensor(half(acc, h), half(acc, h), gated[:, n % 2, :],
                                        ALU.add).then_inc(acc_done, 1)

            nc.gpsimd.memset(zero[:, :].bitcast(f32), 0.0).then_inc(zero_ready, 1)
            nc.gpsimd.memset(ident[:, :], 0.0).then_inc(zeroed, 1)
            nc.gpsimd.memset(neg_half[:, :], -0.5).then_inc(zeroed, 1)
            nc.gpsimd.memset(ones[:, :].bitcast(f32), 1.0).then_inc(consts_ready, 1)
            pool.wait_ge(zeroed, 2)
            nc.gpsimd.affine_select(out=ident[:, :], in_=ident[:, :], compare_op=ALU.not_equal, fill=1.0,
                                    base=0, pattern=[[-1, P]], channel_multiplier=1).then_inc(ident_ready, 1)
            reciprocal_root(0)
            lo_expert(0)
            lo_expert(1)
            reciprocal_root(1)
            lo_expert(2)
            for n in range(STEPS - 1):
                if 3 <= n + 3 < E:
                    lo_expert(n + 3)
                if E + 3 <= n < E + 6:
                    lo_ffn(n - E - 3)
                accumulate(n)
                if n == E + 1:
                    reciprocal_root(HALVES)
            reciprocal_root(HALVES + 1)
            for j in range(BY_POOL):
                lo_prod(j)

        @block.scalar
        def _(act):
            def hi_expert(e):
                act.wait_ge(we_in[e], 16)
                nc.scalar.activation(weh[:, e, :], we[:, e, :], ACT.Copy).then_inc(w_hi, 1)

            def hi_ffn(b):
                if b == 0:
                    act.wait_ge(wf_in, 16)
                c = slice(b * FC * P, (b + 1) * FC * P)
                nc.scalar.activation(wff[:, c], wf[:, c], ACT.Copy).then_inc(w_float, 1)
                nc.scalar.activation(wfh[:, c], wf[:, c], ACT.Copy).then_inc(w_hi, 1)

            def hi_norm(g):
                act.wait_ge(n_turned, g + 1)
                nc.scalar.activation(nh[:, g, :], tr_ps[:, :], ACT.Copy).then_inc(nh_ready, 1)

            def normalise(g):
                act.wait_ge(shift_ready, SHARED.index(g) + 1)
                act.wait_ge(rstd_ready, g + 1)
                if g >= 2:
                    act.wait_ge(n_turned, g - 1)
                for j in range(TPH // 2, TPH):
                    src = xt[:, g * TPH + j, :] if g < HALVES else turned_tile(g - HALVES, j)
                    nc.scalar.activation(xn[:, g % 2, j, :], src, ACT.Identity,
                                         bias=shift[:, g, j - TPH // 2:j - TPH // 2 + 1],
                                         scale=rstd[:, g, j:j + 1]).then_inc(norm_act_ready, 1)

            def gate_copy(n):
                act.wait_ge(gate_done, n + 1)
                if n >= 2:
                    act.wait_ge(gated_ready, n - 1)
                nc.scalar.activation(gbc[:, n % 2, :], gate_ps[:, :], ACT.Copy).then_inc(gbc_ready, 1)

            def hi_hidden(m):
                act.wait_ge(hid_done, m + 1)
                if m >= HR:
                    act.wait_ge(out_done, m - HR + 1)
                nc.scalar.activation(hh[:, m % HR, :], hid[m % HR][:, :], ACT.Relu).then_inc(hh_ready, 1)

            def silu(j):
                act.wait_ge(up_done, 2 * j + 1)
                if j >= 2:
                    act.wait_ge(prod_ready, j - 1)
                nc.scalar.activation(sg[:, j % 2, :], hid[2 * j % HR][:, :], ACT.Silu,
                                     scale=SCALE).then_inc(sg_ready, 1)

            def hi_prod(j):
                act.wait_ge(prod_ready, j + 1)
                nc.scalar.activation(fh[:, j, :], prod[:, j % 2, :], ACT.Copy).then_inc(fh_ready, 1)

            act.wait_ge(consts_ready, 1)
            nc.scalar.activation(warm[:, :], ones[:, 0:1].bitcast(f32), ACT.Silu)
            hi_expert(0)
            normalise(0)
            hi_norm(0)
            hi_expert(1)
            hi_expert(2)
            for m in range(M):
                if m == 9:
                    hi_norm(1)
                if m == 27:
                    hi_norm(2)
                hi_hidden(m)
                if m % 2 == 0:
                    gate_copy(m // 2)
                else:
                    if m // 2 + 3 < E:
                        hi_expert(m // 2 + 3)
                    if E <= m // 2 + 1 < E + 3:
                        hi_ffn(m // 2 + 1 - E)
            silu(0)
            silu(1)
            hi_prod(0)
            hi_prod(1)
            normalise(3)
            silu(2)
            hi_norm(3)
            hi_prod(2)
            for j in range(FC, J):
                silu(j)
                hi_prod(j)

        @block.vector
        def _(dve):
            def layernorm_stats(g):
                if g == 1:
                    dve.wait_ge(x1_in, 16)
                elif g >= HALVES:
                    dve.wait_ge(y_turned, g - HALVES + 1)
                for j in range(TPH):
                    if g == 0 and j % 2 == 0:
                        dve.wait_ge(x0_in[j // 2], 16)
                    src = xt[:, g * TPH + j, :] if g < HALVES else turned_tile(g - HALVES, j)
                    nc.vector.bn_stats(stats[:, g, j, :], src).then_inc(stats_ready, 1)
                for j in range(TPH):
                    dve.wait_ge(stats_ready, g * TPH + j + 1)
                    nc.vector.bn_aggr(mv[:, g, j, :], stats[:, g, j, :]).then_inc(aggr_ready, 1)
                dve.wait_ge(aggr_ready, (g + 1) * TPH)
                nc.vector.tensor_scalar(veps[:, g, :], mv[:, g, :, 1], EPS, None, ALU.add).then_inc(veps_ready, 1)

            def normalise(g):
                dve.wait_ge(rstd_ready, g + 1)
                if g >= 2:
                    dve.wait_ge(n_turned, g - 1)
                tiles = range(TPH)
                if g in SHARED:
                    tiles = range(TPH // 2)
                    nc.vector.scalar_tensor_tensor(out=shift[:, g, :], in0=mv[:, g, TPH // 2:, 0], scalar=-1.0,
                                                   in1=rstd[:, g, TPH // 2:], op0=ALU.mult,
                                                   op1=ALU.mult).then_inc(shift_ready, 1)
                for j in tiles:
                    src = xt[:, g * TPH + j, :] if g < HALVES else turned_tile(g - HALVES, j)
                    nc.vector.tensor_scalar(xn[:, g % 2, j, :], src, mv[:, g, j, 0:1], rstd[:, g, j:j + 1],
                                            ALU.subtract, ALU.mult).then_inc(norm_ready, 1)

            def lo_norm(g):
                dve.wait_ge(nh_ready, g + 1)
                nc.vector.tensor_tensor(nl[:, g, :], tr_ps[:, :], nh[:, g, :].bitcast(f32),
                                        ALU.subtract).then_inc(nl_ready, 1)

            def split_routing(h):
                dve.wait_ge(cw_in[h], 16)
                nc.vector.tensor_copy(half(chl, h), half(cw, h)).then_inc(chi_ready, 1)
                dve.wait_ge(chi_ready, h + 1)
                low = chl[P // 2:P, h * N:(h + 1) * N]
                nc.vector.tensor_tensor(low, cw[P // 2:P, h * N:(h + 1) * N], low.bitcast(f32),
                                        ALU.subtract).then_inc(chl_ready, 1)

            def mask(n):
                h = n // E
                if n % E == 0:
                    dve.wait_ge(ids_in[h], 16)
                    dve.wait_ge(chl_ready, h + 1)
                if n >= MR:
                    dve.wait_ge(gate_done, n - MR + 1)
                nc.vector.scalar_tensor_tensor(out=msk[:, n % MR, :], in0=half(ids, h), scalar=float(n % E),
                                               in1=half(chl, h).bitcast(f32),
                                               op0=ALU.is_equal, op1=ALU.mult).then_inc(mask_ready, 1)

            def lo_hidden(m):
                dve.wait_ge(hh_ready, m + 1)
                nc.vector.scalar_tensor_tensor(out=hl[:, m % HR, :], in0=hid[m % HR][:, :], scalar=0.0,
                                               in1=hh[:, m % HR, :].bitcast(f32),
                                               op0=ALU.max, op1=ALU.subtract).then_inc(hl_ready, 1)

            def apply_gate(n):
                dve.wait_ge(out_done, 2 * n + 2)
                dve.wait_ge(gbc_ready, n + 1)
                if n >= 2:
                    dve.wait_ge(acc_done, n - 1)
                nc.vector.tensor_tensor(gated[:, n % 2, :], outp[n % 2][:, :], gbc[:, n % 2, :],
                                        ALU.mult).then_inc(gated_ready, 1)

            def accumulate_last():
                dve.wait_ge(acc_done, STEPS - 1)
                dve.wait_ge(gated_ready, STEPS)
                nc.vector.tensor_tensor(half(acc, 1), half(acc, 1), gated[:, (STEPS - 1) % 2, :],
                                        ALU.add).then_inc(acc_last, 1)

            def multiply(j):
                dve.wait_ge(up_done, 2 * j + 2)
                dve.wait_ge(sg_ready, j + 1)
                if j >= 2:
                    if j - 2 < BY_POOL:
                        dve.wait_ge(fl_pool_ready, j - 1)
                    else:
                        dve.wait_ge(fl_ready, j - 1 - BY_POOL)
                nc.vector.tensor_tensor(prod[:, j % 2, :], hid[(2 * j + 1) % HR][:, :], sg[:, j % 2, :],
                                        ALU.mult).then_inc(prod_ready, 1)

            def lo_prod(j):
                dve.wait_ge(fh_ready, j + 1)
                nc.vector.tensor_tensor(fl[:, j, :], prod[:, j % 2, :], fh[:, j, :].bitcast(f32),
                                        ALU.subtract).then_inc(fl_ready, 1)

            def finish(h):
                dve.wait_ge(down_done, FC * (h + 1))
                nc.vector.scalar_tensor_tensor(out=half(res, h), in0=outp[h][:, :], scalar=SCALE * SCALE,
                                               in1=half(acc, h), op0=ALU.mult, op1=ALU.add).then_inc(res_ready, 1)

            layernorm_stats(0)
            normalise(0)
            split_routing(0)
            mask(0)
            lo_norm(0)
            mask(1)
            layernorm_stats(1)
            for m in range(M):
                if m == 5:
                    normalise(1)
                if m == 9:
                    lo_norm(1)
                if m == 11:
                    split_routing(1)
                if m == 20:
                    layernorm_stats(2)
                if m == 24:
                    normalise(2)
                if m == 27:
                    lo_norm(2)
                lo_hidden(m)
                if m % 2 == 0:
                    if m // 2 + 2 < STEPS:
                        mask(m // 2 + 2)
                elif m >= 3:
                    apply_gate((m - 3) // 2)
            apply_gate(STEPS - 1)
            accumulate_last()
            layernorm_stats(3)
            multiply(0)
            multiply(1)
            normalise(3)
            multiply(2)
            lo_norm(3)
            lo_prod(2)
            for j in range(FC, J):
                multiply(j)
                lo_prod(j)
                if j == FC:
                    finish(0)
            finish(1)

        @block.tensor
        def _(pe):
            def turn_norm(g):
                if g == 0:
                    pe.wait_ge(ident_ready, 1)
                else:
                    pe.wait_ge(nl_ready, g)
                done = sum(TPH // 2 if i in SHARED else TPH for i in range(g + 1))
                pe.wait_ge(norm_ready, done)
                if g in SHARED:
                    pe.wait_ge(norm_act_ready, TPH // 2 * (SHARED.index(g) + 1))
                for j in range(TPH):
                    last = nc.tensor.transpose(tr_ps[:, j * P:(j + 1) * P], xn[:, g % 2, j, :], ident[:, :])
                last.then_inc(n_turned, 1)

            def turn_y(h):
                pe.wait_ge(nl_ready, HALVES + h)
                if h == HALVES - 1:
                    pe.wait_ge(gbc_ready, STEPS)
                if h == 0:
                    pe.wait_ge(acc_done, E)
                else:
                    pe.wait_ge(acc_last, 1)
                for j in range(TPH):
                    c = h * N + j * P
                    last = nc.tensor.transpose(turned_tile(h, j), acc[:, c:c + P], ident[:, :])
                last.then_inc(y_turned, 1)

            def gate(n):
                if n == 0:
                    pe.wait_ge(consts_ready, 1)
                else:
                    pe.wait_ge(gbc_ready, n)
                pe.wait_ge(mask_ready, n + 1)
                nc.tensor.matmul(gate_ps[:, :], ones[:, :], msk[:, n % MR, :],
                                 start=True, stop=True).then_inc(gate_done, 1)

            def warm_up():
                pe.wait_ge(zero_ready, 1)
                for _ in range(WARM):
                    nc.tensor.matmul(outp[1][:, :], zero[:, 0:P], zero[:, :], start=True, stop=True)

            def by_hi(dst, wh, wl, xh, start=True):
                nc.tensor.matmul(dst, wh, xh, start=start, stop=False)
                nc.tensor.matmul(dst, wl, xh, start=False, stop=False)

            def by_lo(dst, wh, xl, stop=True):
                return nc.tensor.matmul(dst, wh, xl, start=False, stop=stop)

            def first_product(m):
                n, c = m // CH, m % CH
                h, e = n // E, n % E
                if c == 0 and h == 0:
                    pe.wait_ge(w_lo, e + 1)
                if m % (M // HALVES) == 0:
                    pe.wait_ge(nh_ready, h + 1)
                if m >= HR:
                    pe.wait_ge(hl_ready, m - HR + 1)
                w = slice(c * P, (c + 1) * P)
                by_hi(hid[m % HR][:, :], weh[:, e, w], wel[:, e, w], nh[:, h, :])
                if m % (M // HALVES) == 0:
                    pe.wait_ge(nl_ready, h + 1)
                by_lo(hid[m % HR][:, :], weh[:, e, w], nl[:, h, :]).then_inc(hid_done, 1)

            def second_product(m):
                n, c = m // CH, m % CH
                e = n % E
                if c == 0 and n >= 2:
                    pe.wait_ge(gated_ready, n - 1)
                pe.wait_ge(hh_ready, m + 1)
                w = slice((CH + c) * P, (CH + c + 1) * P)
                by_hi(outp[n % 2][:, :], weh[:, e, w], wel[:, e, w], hh[:, m % HR, :], start=(c == 0))
                pe.wait_ge(hl_ready, m + 1)
                by_lo(outp[n % 2][:, :], weh[:, e, w], hl[:, m % HR, :], stop=(c == CH - 1)).then_inc(out_done, 1)

            def gate_up(j):
                h, c = j // FC, j % FC
                if j < 2:
                    pe.wait_ge(hl_ready, M - 2 + 2 * j)
                else:
                    pe.wait_ge(prod_ready, j - 1)
                if j == 0:
                    pe.wait_ge(w_lo, E + 3)
                g = HALVES + h
                if c == 0:
                    pe.wait_ge(nh_ready, g + 1)
                    pe.wait_ge(nl_ready, g + 1)
                for b in range(2):
                    w = slice((b * FC + c) * P, (b * FC + c + 1) * P)
                    by_hi(hid[(2 * j + b) % HR][:, :], wfh[:, w], wfl[:, w], nh[:, g, :])
                    by_lo(hid[(2 * j + b) % HR][:, :], wfh[:, w], nl[:, g, :]).then_inc(up_done, 1)

            def down(j):
                h, c = j // FC, j % FC
                if c == 0:
                    pe.wait_ge(gated_ready, STEPS - 1 + h)
                w = slice((2 * FC + c) * P, (2 * FC + c + 1) * P)
                pe.wait_ge(fh_ready, j + 1)
                by_hi(outp[h][:, :], wfh[:, w], wfl[:, w], fh[:, j, :], start=(c == 0))
                if j < BY_POOL:
                    pe.wait_ge(fl_pool_ready, j + 1)
                else:
                    pe.wait_ge(fl_ready, j - BY_POOL + 1)
                by_lo(outp[h][:, :], wfh[:, w], fl[:, j, :], stop=(c == FC - 1)).then_inc(down_done, 1)

            warm_up()
            turn_norm(0)
            for m in range(M + LAG):
                if m == 8:
                    turn_norm(1)
                if m == 20:
                    turn_y(0)
                if m == 26:
                    turn_norm(2)
                if m < M:
                    first_product(m)
                    if m % CH == 0:
                        gate(m // CH)
                if m >= LAG:
                    second_product(m - LAG)
            gate_up(0)
            gate_up(1)
            turn_y(1)
            gate_up(2)
            down(0)
            down(1)
            turn_norm(3)
            down(2)
            gate_up(3)
            gate_up(4)
            gate_up(5)
            down(3)
            down(4)
            down(5)


def kernel(x, ctx_512, itok_BxS2xS_0_7, L0_xattn_proj_in, L0_xattn_proj_out,
           L0_ffn_w_gate, L0_ffn_w_up, L0_ffn_w_down):
    import numpy as np
    import concourse.bacc as bacc
    from concourse import mybir
    from concourse.bass_utils import run_bass_kernel_spmd

    P = 128
    x = np.asarray(x)
    B, S, D = x.shape
    T = B * S
    win, wout = np.asarray(L0_xattn_proj_in), np.asarray(L0_xattn_proj_out)
    E, HID, _ = win.shape
    CH = HID // P
    rows = x.reshape(T, D)
    w_experts = np.concatenate(
        [win.transpose(2, 0, 1), wout.reshape(E, D, CH, P).transpose(3, 0, 2, 1).reshape(P, E, CH * D)], axis=2)
    down = np.asarray(L0_ffn_w_down).T
    w_ffn = np.concatenate(
        [np.asarray(L0_ffn_w_gate).T, np.asarray(L0_ffn_w_up).T,
         down.reshape(-1, P, D).transpose(1, 0, 2).reshape(P, -1)], axis=1)
    def choices_first(a):
        a = np.asarray(a).transpose(1, 0, 2).reshape(-1, T)
        return np.concatenate([a, a], axis=0)

    arrays = {
        "x_tok": rows.reshape(T // P, P, D).transpose(1, 0, 2),
        "x_feat": rows.T,
        "ctx_kt": choices_first(ctx_512),
        "ids_kt": choices_first(itok_BxS2xS_0_7),
        "w_experts": w_experts,
        "w_ffn": w_ffn,
    }
    arrays = {k: np.ascontiguousarray(v) for k, v in arrays.items()}
    nc = bacc.Bacc("TRN2", target_bir_lowering=False, num_devices=1)
    ins = [nc.dram_tensor(k, v.shape, mybir.dt.from_np(v.dtype), kind="ExternalInput").ap()
           for k, v in arrays.items()]
    out = nc.dram_tensor("out_feat", (D, T), mybir.dt.float32, kind="ExternalOutput").ap()
    xattn_ffn_program(nc, *ins, out)
    r = run_bass_kernel_spmd(nc, [arrays], core_ids=[0])
    return np.ascontiguousarray(r.results[0]["out_feat"].T).reshape(B, S, D)
```

```python
import concourse.bass as bass
from concourse import mybir
from contextlib import ExitStack


def xattn_ffn_program(
    nc: bass.Bass,
    x_tok: bass.AP,
    x_feat: bass.AP,
    ctx_kt: bass.AP,
    ids_kt: bass.AP,
    w_experts: bass.AP,
    w_ffn: bass.AP,
    out_feat: bass.AP,
):
    f32 = mybir.dt.float32
    f32r = mybir.dt.float32r
    i32 = mybir.dt.int32
    ALU = mybir.AluOpType
    ACT = mybir.ActivationFunctionType

    P = 128
    E = w_experts.shape[1]
    T = x_feat.shape[1]
    N = 512
    Q = N // 2
    HALVES = T // N
    TILES = T // P
    TPH = N // P
    STEPS = HALVES * E
    CH = w_experts.shape[2] // 2 // P
    M = STEPS * CH
    HR = 4
    LAG = 3
    SPARE = (M - CH) % HR
    PR = 6
    MR = 3
    FC = w_ffn.shape[1] // 3 // P
    QUARTERS = T // Q
    K = QUARTERS * FC
    HI_BY_DVE = (K - 2, K - 1)
    BY_POOL = (0, 1, 2, 3, 4, 5, 7, 9)
    GROUPS = [range(0, 2), range(2, TPH), range(TPH, TILES), range(TILES, TILES + TPH),
              range(TILES + TPH, TILES + TPH + 2), range(TILES + TPH + 2, 2 * TILES)]
    BEHIND = 3
    OTHER_BANK = (1, 5)
    BY_DVE = 2
    MASK_BY_POOL = 2
    ROUTING_AT = 4
    WARM = 10
    EPS = 1e-5
    SCALE = 1.0 / 127.0

    with ExitStack() as ctx:
        def sb(name, shape, dt=f32):
            return ctx.enter_context(nc.sbuf_tensor(name, shape, dt))

        def bank(name):
            return ctx.enter_context(nc.psum_tensor(name, [P, N], f32))

        def sem(name):
            return ctx.enter_context(nc.semaphore(name))

        xt = sb("xt", [P, TILES, P])
        acc = sb("acc", [P, T])
        cw = sb("cw", [P, T])
        ids = sb("ids", [P, T], i32)
        we = sb("we", [P, E, 2 * CH * P])
        wf = sb("wf", [P, 3 * FC * P], i32)
        ident = sb("ident", [P, P])
        ones = sb("ones", [P, P], f32r)
        zero = sb("zero", [P, N], f32r)
        neg_half = sb("neg_half", [P, TPH])
        table = sb("table", [P, 1])
        stats = sb("stats", [P, 2 * TILES, 6])
        mv = sb("mv", [P, 2 * TILES, 2])
        veps = sb("veps", [P, 2 * TILES])
        rstd = sb("rstd", [P, 2 * TILES])
        shift = sb("shift", [P, 2 * TILES])
        xn = sb("xn", [P, 2 * TILES, P])
        nh = sb("nh", [P, 2 * T], f32r)
        nl = sb("nl", [P, 2 * T], f32r)
        weh = sb("weh", [P, E, 2 * CH * P], f32r)
        wel = sb("wel", [P, E, 2 * CH * P], f32r)
        wff = sb("wff", [P, 3 * FC * P])
        wfh = sb("wfh", [P, 3 * FC * P], f32r)
        wfl = sb("wfl", [P, 3 * FC * P], f32r)
        chl = sb("chl", [P, T], f32r)
        named = sb("named", [P, N])
        msk = sb("msk", [P, MR, N], f32r)
        gbc = sb("gbc", [P, 2, N])
        gated = sb("gated", [P, 2, N])
        hh = sb("hh", [P, HR, N], f32r)
        hl = sb("hl", [P, HR, N], f32r)
        sg = sb("sg", [P, HR, Q])
        prod = sb("prod", [P, PR, Q])
        fh = sb("fh", [P, K, Q], f32r)
        fl = sb("fl", [P, K, Q], f32r)
        res = sb("res", [P, T])

        hid = [bank(f"hid{i}") for i in range(HR)]
        outp = [bank(f"outp{i}") for i in range(2)]
        gate_ps = bank("gate_ps")
        tr_ps = bank("tr_ps")

        x0_in = [sem(f"x0_in{i}") for i in range(2)]
        x1_in = sem("x1_in")
        cw_in = [sem(f"cw_in{h}") for h in range(HALVES)]
        ids_in = [sem(f"ids_in{h}") for h in range(HALVES)]
        we_in = [sem(f"we_in{e}") for e in range(E)]
        wf_in = sem("wf_in")
        acc_in = sem("acc_in")
        zero_ready = sem("zero_ready")
        zeroed = sem("zeroed")
        ones_ready = sem("ones_ready")
        ident_ready = sem("ident_ready")
        stats_ready = sem("stats_ready")
        aggr_ready = sem("aggr_ready")
        veps_ready = sem("veps_ready")
        rstd_ready = sem("rstd_ready")
        shift_ready = sem("shift_ready")
        y_turned = sem("y_turned")
        n_turned = sem("n_turned")
        norm_ready = sem("norm_ready")
        norm_act_ready = sem("norm_act_ready")
        nh_ready = sem("nh_ready")
        nl_ready = sem("nl_ready")
        w_float = sem("w_float")
        w_hi = sem("w_hi")
        w_lo = sem("w_lo")
        chi_ready = sem("chi_ready")
        chl_ready = sem("chl_ready")
        mask_ready = sem("mask_ready")
        named_ready = sem("named_ready")
        mask_pool_ready = sem("mask_pool_ready")
        gate_done = sem("gate_done")
        gbc_ready = sem("gbc_ready")
        hid_done = sem("hid_done")
        hh_ready = sem("hh_ready")
        hl_ready = sem("hl_ready")
        out_done = sem("out_done")
        gated_ready = sem("gated_ready")
        acc_done = sem("acc_done")
        acc_last = sem("acc_last")
        up_done = sem("up_done")
        sg_ready = sem("sg_ready")
        prod_ready = sem("prod_ready")
        fh_ready = sem("fh_ready")
        fh_dve_ready = sem("fh_dve_ready")
        fl_pool_ready = sem("fl_pool_ready")
        fl_ready = sem("fl_ready")
        down_done = sem("down_done")
        sum_scaled = sem("sum_scaled")
        res_ready = sem("res_ready")
        res_last = sem("res_last")
        stored = sem("stored")

        block = ctx.enter_context(nc.Block())

        def half(t, h):
            return t[:, h * N:(h + 1) * N]

        def quarter(t, q):
            return t[:, q * Q:(q + 1) * Q]

        def group_cols(g):
            return slice(GROUPS[g].start * P, GROUPS[g].stop * P)

        def group_bank(g):
            return gate_ps if g in OTHER_BANK else tr_ps

        def step_sum(n, c=slice(0, N)):
            return hid[SPARE][:, 0:Q] if (n == STEPS - 1 and c.start > 0) else outp[n % 2][:, c]

        def turned_tile(g, i):
            b = i - GROUPS[g].start
            return group_bank(g)[:, b * P:(b + 1) * P]

        def ffn_block(b):
            return slice(b * FC * P, (b + 1) * FC * P)

        def hi_taken(engine, k):
            if k in HI_BY_DVE:
                engine.wait_ge(fh_dve_ready, HI_BY_DVE.index(k) + 1)
            else:
                engine.wait_ge(fh_ready, k + 1)

        def lo_taken(engine, k):
            by_pool = sum(1 for j in BY_POOL if j <= k)
            if k in BY_POOL:
                engine.wait_ge(fl_pool_ready, by_pool)
            else:
                engine.wait_ge(fl_ready, k + 1 - by_pool)

        @block.sync
        def _(sp):
            def load_weights_of_choices(h):
                sp.dma_start(half(cw, h), half(ctx_kt, h)).then_inc(cw_in[h], 16)

            def load_choices(h):
                sp.dma_start(half(ids, h), half(ids_kt, h)).then_inc(ids_in[h], 16)

            def load_expert(e):
                sp.dma_start(we[:, e, :], w_experts[:, e, :]).then_inc(we_in[e], 16)

            for i in range(2):
                sp.dma_start(xt[:, 2 * i:2 * i + 2, :], x_tok[:, 2 * i:2 * i + 2, :]).then_inc(x0_in[i], 16)
            load_expert(0)
            load_expert(1)
            load_weights_of_choices(0)
            load_expert(2)
            load_choices(0)
            sp.dma_start(xt[:, TPH:TILES, :], x_tok[:, TPH:TILES, :]).then_inc(x1_in, 16)
            load_expert(3)
            sp.dma_start(acc[:, :], x_feat).then_inc(acc_in, 16)
            for e in range(4, E):
                load_expert(e)
            load_weights_of_choices(1)
            load_choices(1)
            sp.dma_start(wf[:, :], w_ffn).then_inc(wf_in, 16)
            for q in range(QUARTERS):
                if q < QUARTERS - 1:
                    sp.wait_ge(res_ready, q + 1)
                else:
                    sp.wait_ge(res_last, 1)
                sp.dma_start(quarter(out_feat, q), quarter(res, q)).then_inc(stored, 16)
            sp.wait_ge(stored, 16 * QUARTERS)

        @block.gpsimd
        def _(pool):
            def lo_expert(e):
                pool.wait_ge(w_hi, e + 1)
                for parts in ((0, 1), (1, 2)) if e < 2 else ((0, 2),):
                    c = slice(parts[0] * CH * P, parts[1] * CH * P)
                    nc.gpsimd.tensor_tensor(wel[:, e, c], we[:, e, c], weh[:, e, c].bitcast(f32),
                                            ALU.subtract).then_inc(w_lo, parts[1] - parts[0])

            def lo_routing(h):
                pool.wait_ge(acc_done, ROUTING_AT + 1)
                pool.wait_ge(chi_ready, h + 1)
                low = half(chl, h)[P // 2:P, :]
                nc.gpsimd.tensor_tensor(low, half(cw, h)[P // 2:P, :], low.bitcast(f32),
                                        ALU.subtract).then_inc(chl_ready, 1)

            def mask_in_two(n):
                pool.wait_ge(ids_in[0], 16)
                pool.wait_ge(chl_ready, 1)
                nc.gpsimd.tensor_scalar(named[:, :], half(ids, 0), float(n), None,
                                        ALU.is_equal).then_inc(named_ready, 1)
                pool.wait_ge(named_ready, 1)
                nc.gpsimd.tensor_tensor(msk[:, n % MR, :], half(chl, 0).bitcast(f32), named[:, :],
                                        ALU.mult).then_inc(mask_pool_ready, 1)

            def lo_ffn(b):
                pool.wait_ge(w_float, b + 1)
                pool.wait_ge(w_hi, E + b + 1)
                c = ffn_block(b)
                nc.gpsimd.tensor_tensor(wfl[:, c], wff[:, c], wfh[:, c].bitcast(f32),
                                        ALU.subtract).then_inc(w_lo, 1)

            def reciprocal_root(g):
                pool.wait_ge(veps_ready, g + 1)
                r = slice(GROUPS[g].start, GROUPS[g].stop)
                nc.gpsimd.tensor_tensor(rstd[:, r], veps[:, r], neg_half[:, 0:len(GROUPS[g])],
                                        ALU.pow).then_inc(rstd_ready, 1)

            def accumulate(n, c=slice(0, N)):
                if n == 0:
                    pool.wait_ge(acc_in, 16)
                else:
                    pool.wait_ge(acc_done, n)
                if n == ROUTING_AT + 1:
                    pool.wait_ge(chl_ready, HALVES)
                pool.wait_ge(gated_ready, n + 1)
                a = half(acc, n // E)[:, c]
                nc.gpsimd.tensor_tensor(a, a, gated[:, n % 2, c], ALU.add).then_inc(acc_done, 1)

            def lo_prod(k):
                pool.wait_ge(fh_ready, k + 1)
                nc.gpsimd.tensor_tensor(fl[:, k, :], prod[:, k % PR, :], fh[:, k, :].bitcast(f32),
                                        ALU.subtract).then_inc(fl_pool_ready, 1)

            def add_rest(q):
                pool.wait_ge(sum_scaled, q + 1)
                nc.gpsimd.tensor_tensor(quarter(res, q), quarter(res, q), quarter(acc, q),
                                        ALU.add).then_inc(res_ready, 1)

            nc.gpsimd.memset(zero[:, :].bitcast(f32), 0.0).then_inc(zero_ready, 1)
            nc.gpsimd.memset(ident[:, :], 0.0).then_inc(zeroed, 1)
            nc.gpsimd.memset(neg_half[:, :], -0.5).then_inc(zeroed, 1)
            nc.gpsimd.memset(ones[:, :].bitcast(f32), 1.0).then_inc(ones_ready, 1)
            pool.wait_ge(zeroed, 2)
            nc.gpsimd.affine_select(out=ident[:, :], in_=ident[:, :], compare_op=ALU.not_equal, fill=1.0,
                                    base=0, pattern=[[-1, P]], channel_multiplier=1).then_inc(ident_ready, 1)
            reciprocal_root(0)
            reciprocal_root(1)
            for e in range(3):
                lo_expert(e)
            for n in range(STEPS - 1):
                if n == 0:
                    lo_expert(3)
                    lo_expert(4)
                    mask_in_two(MASK_BY_POOL)
                    reciprocal_root(2)
                elif n + 4 < E:
                    lo_expert(n + 4)
                if E + 3 <= n < E + 6:
                    lo_ffn(n - E - 3)
                accumulate(n, slice(0, N) if n < STEPS - 2 else slice(Q, N))
                if n == ROUTING_AT:
                    lo_routing(1)
                if n == E:
                    reciprocal_root(3)
            pool.wait_ge(gated_ready, STEPS + 1)
            accumulate(STEPS - 1, slice(Q, N))
            for k in BY_POOL:
                if k in (0, 1):
                    reciprocal_root(4 + k)
                lo_prod(k)
                if k in (7, 9):
                    add_rest((k - 7) // 2)
            add_rest(2)

        @block.scalar
        def _(act):
            def hi_expert(e):
                act.wait_ge(we_in[e], 16)
                nc.scalar.activation(weh[:, e, :], we[:, e, :], ACT.Copy).then_inc(w_hi, 1)

            def float_ffn(b):
                act.wait_ge(wf_in, 16)
                c = ffn_block(b)
                nc.scalar.activation(wff[:, c], wf[:, c], ACT.Copy).then_inc(w_float, 1)

            def hi_ffn(b):
                act.wait_ge(wf_in, 16)
                c = ffn_block(b)
                nc.scalar.activation(wfh[:, c], wf[:, c], ACT.Copy).then_inc(w_hi, 1)

            def hi_routing(h):
                act.wait_ge(cw_in[h], 16)
                nc.scalar.activation(half(chl, h), half(cw, h), ACT.Copy).then_inc(chi_ready, 1)

            def normalise(g, j):
                act.wait_ge(shift_ready, g - BY_DVE + 1)
                act.wait_ge(rstd_ready, g + 1)
                i = GROUPS[g][j]
                src = xt[:, i, :] if i < TILES else turned_tile(g, i)
                nc.scalar.activation(xn[:, i, :], src, ACT.Identity, bias=shift[:, i:i + 1],
                                     scale=rstd[:, i:i + 1]).then_inc(norm_act_ready, 1)

            def hi_norm(g):
                act.wait_ge(n_turned, g + 1)
                c = group_cols(g)
                nc.scalar.activation(nh[:, c], group_bank(g)[:, 0:c.stop - c.start],
                                     ACT.Copy).then_inc(nh_ready, 1)

            def gate_copy(n):
                act.wait_ge(gate_done, n + 1)
                if n >= 2:
                    act.wait_ge(gated_ready, n - 1)
                nc.scalar.activation(gbc[:, n % 2, :], gate_ps[:, :], ACT.Copy).then_inc(gbc_ready, 1)

            def hi_hidden(m):
                act.wait_ge(hid_done, m + 1)
                if m >= HR:
                    act.wait_ge(out_done, m - HR + 1)
                nc.scalar.activation(hh[:, m % HR, :], hid[m % HR][:, :], ACT.Relu).then_inc(hh_ready, 1)

            def silu(k):
                act.wait_ge(up_done, k + 1)
                if k >= HR:
                    act.wait_ge(prod_ready, k - HR + 1)
                nc.scalar.activation(sg[:, k % HR, :], hid[k % HR][:, 0:Q], ACT.Silu,
                                     scale=SCALE).then_inc(sg_ready, 1)

            def hi_prod(k):
                act.wait_ge(prod_ready, k + 1)
                nc.scalar.activation(fh[:, k, :], prod[:, k % PR, :], ACT.Copy).then_inc(fh_ready, 1)

            def scale_sum(q):
                act.wait_ge(down_done, FC * (q + 1))
                nc.scalar.activation(quarter(res, q), outp[q % 2][:, 0:Q], ACT.Copy,
                                     scale=SCALE * SCALE).then_inc(sum_scaled, 1)

            act.wait_ge(ones_ready, 1)
            nc.scalar.activation(table[:, :], ones[:, 0:1].bitcast(f32), ACT.Silu)
            hi_expert(0)
            hi_expert(1)
            hi_norm(0)
            hi_norm(1)
            hi_expert(2)
            for m in range(M):
                n = m // CH
                if m == 14:
                    hi_norm(2)
                if m == 30:
                    hi_norm(3)
                hi_hidden(m)
                if 9 <= m < 9 + TPH:
                    normalise(2, m - 9)
                if 25 <= m < 25 + TPH:
                    normalise(3, m - 25)
                if m % CH:
                    if n >= 1:
                        gate_copy(n - 1)
                    if E - 1 <= n < E + 2:
                        float_ffn(n + 1 - E)
                    if n == 0:
                        hi_expert(3)
                else:
                    if 1 <= n and n + 3 < E:
                        hi_expert(n + 3)
                    if n == ROUTING_AT:
                        hi_routing(1)
                    if E <= n < E + 3:
                        hi_ffn(n - E)
            gate_copy(STEPS - 1)
            silu(0)
            silu(1)
            hi_prod(0)
            silu(2)
            hi_prod(1)
            normalise(4, 0)
            normalise(4, 1)
            silu(3)
            hi_prod(2)
            hi_norm(4)
            normalise(5, 0)
            normalise(5, 1)
            silu(4)
            hi_prod(3)
            hi_norm(5)
            silu(5)
            hi_prod(4)
            for k in range(6, K):
                silu(k)
                if k - 1 not in HI_BY_DVE:
                    hi_prod(k - 1)
                if k in (8, 10):
                    scale_sum((k - 8) // 2)
            scale_sum(2)

        @block.vector
        def _(dve):
            def layernorm_stats(g, part=None):
                if g >= BEHIND:
                    dve.wait_ge(y_turned, g - BEHIND + 1)
                else:
                    dve.wait_ge((*x0_in, x1_in)[g], 16)
                tiles = GROUPS[g] if part is None else GROUPS[g][2 * part:2 * part + 2]
                for i in tiles:
                    src = xt[:, i, :] if i < TILES else turned_tile(g, i)
                    nc.vector.bn_stats(stats[:, i, :], src).then_inc(stats_ready, 1)
                for i in tiles:
                    dve.wait_ge(stats_ready, i + 1)
                    nc.vector.bn_aggr(mv[:, i, :], stats[:, i, :]).then_inc(aggr_ready, 1)
                if part == 0:
                    return
                dve.wait_ge(aggr_ready, GROUPS[g].stop)
                r = slice(GROUPS[g].start, GROUPS[g].stop)
                nc.vector.tensor_scalar(veps[:, r], mv[:, r, 1], EPS, None, ALU.add).then_inc(veps_ready, 1)

            def normalise(g):
                dve.wait_ge(rstd_ready, g + 1)
                for i in GROUPS[g]:
                    nc.vector.tensor_scalar(xn[:, i, :], xt[:, i, :], mv[:, i, 0:1], rstd[:, i:i + 1],
                                            ALU.subtract, ALU.mult).then_inc(norm_ready, 1)

            def shift_for_act(g):
                dve.wait_ge(rstd_ready, g + 1)
                r = slice(GROUPS[g].start, GROUPS[g].stop)
                nc.vector.scalar_tensor_tensor(out=shift[:, r], in0=mv[:, r, 0], scalar=-1.0, in1=rstd[:, r],
                                               op0=ALU.mult, op1=ALU.mult).then_inc(shift_ready, 1)

            def lo_norm(g):
                dve.wait_ge(nh_ready, g + 1)
                c = group_cols(g)
                nc.vector.tensor_tensor(nl[:, c], group_bank(g)[:, 0:c.stop - c.start], nh[:, c].bitcast(f32),
                                        ALU.subtract).then_inc(nl_ready, 1)

            def split_routing(h):
                dve.wait_ge(cw_in[h], 16)
                nc.vector.tensor_copy(half(chl, h), half(cw, h)).then_inc(chi_ready, 1)
                dve.wait_ge(chi_ready, h + 1)
                low = half(chl, h)[P // 2:P, :]
                nc.vector.tensor_tensor(low, half(cw, h)[P // 2:P, :], low.bitcast(f32),
                                        ALU.subtract).then_inc(chl_ready, 1)

            def mask(n):
                h = n // E
                if n % E == 0:
                    dve.wait_ge(ids_in[h], 16)
                    dve.wait_ge(chl_ready, h + 1)
                if n >= MR:
                    dve.wait_ge(gate_done, n - MR + 1)
                nc.vector.scalar_tensor_tensor(out=msk[:, n % MR, :], in0=half(ids, h), scalar=float(n % E),
                                               in1=half(chl, h).bitcast(f32),
                                               op0=ALU.is_equal, op1=ALU.mult).then_inc(mask_ready, 1)

            def lo_hidden(m):
                dve.wait_ge(hh_ready, m + 1)
                nc.vector.scalar_tensor_tensor(out=hl[:, m % HR, :], in0=hid[m % HR][:, :], scalar=0.0,
                                               in1=hh[:, m % HR, :].bitcast(f32),
                                               op0=ALU.max, op1=ALU.subtract).then_inc(hl_ready, 1)

            def apply_gate(n, c=slice(0, N)):
                dve.wait_ge(out_done, CH * (n + 1) - (1 if n == STEPS - 1 and c.start == 0 else 0))
                dve.wait_ge(gbc_ready, n + 1)
                if n >= 2:
                    dve.wait_ge(acc_done, n - 1)
                nc.vector.tensor_tensor(gated[:, n % 2, c], step_sum(n, c), gbc[:, n % 2, c],
                                        ALU.mult).then_inc(gated_ready, 1)

            def accumulate(n, c):
                a = half(acc, n // E)[:, c]
                nc.vector.tensor_tensor(a, a, gated[:, n % 2, c], ALU.add).then_inc(acc_last, 1)

            def multiply(k):
                dve.wait_ge(sg_ready, k + 1)
                if k >= PR:
                    lo_taken(dve, k - PR)
                nc.vector.tensor_tensor(prod[:, k % PR, :], hid[k % HR][:, Q:N], sg[:, k % HR, :],
                                        ALU.mult).then_inc(prod_ready, 1)

            def lo_prod(k):
                if k in HI_BY_DVE:
                    dve.wait_ge(prod_ready, k + 1)
                    nc.vector.tensor_copy(fh[:, k, :], prod[:, k % PR, :]).then_inc(fh_dve_ready, 1)
                hi_taken(dve, k)
                nc.vector.tensor_tensor(fl[:, k, :], prod[:, k % PR, :], fh[:, k, :].bitcast(f32),
                                        ALU.subtract).then_inc(fl_ready, 1)

            def finish(q):
                dve.wait_ge(down_done, FC * (q + 1))
                nc.vector.scalar_tensor_tensor(out=quarter(res, q), in0=outp[q % 2][:, 0:Q],
                                               scalar=SCALE * SCALE, in1=quarter(acc, q),
                                               op0=ALU.mult, op1=ALU.add).then_inc(res_last, 1)

            left, right = slice(0, Q), slice(Q, N)
            layernorm_stats(0)
            layernorm_stats(1)
            normalise(0)
            normalise(1)
            lo_norm(0)
            lo_norm(1)
            split_routing(0)
            for m in range(M):
                if m in (4, 5):
                    layernorm_stats(2, m - 4)
                if m == 7:
                    shift_for_act(2)
                if m == 14:
                    lo_norm(2)
                if m == 31:
                    lo_norm(3)
                if m in (22, 23):
                    layernorm_stats(3, m - 22)
                if m == 25:
                    shift_for_act(3)
                lo_hidden(m)
                if m == 0:
                    mask(0)
                if m % CH:
                    if m < M - 1 and m // CH + 1 != MASK_BY_POOL:
                        mask(m // CH + 1)
                elif m > LAG:
                    apply_gate((m - LAG) // CH)
            apply_gate(STEPS - 2)
            dve.wait_ge(acc_done, STEPS - 2)
            dve.wait_ge(gated_ready, STEPS - 1)
            accumulate(STEPS - 2, left)
            apply_gate(STEPS - 1, left)
            apply_gate(STEPS - 1, right)
            dve.wait_ge(acc_last, 1)
            dve.wait_ge(gated_ready, STEPS)
            accumulate(STEPS - 1, left)
            multiply(0)
            layernorm_stats(4)
            multiply(1)
            layernorm_stats(5)
            shift_for_act(4)
            multiply(2)
            shift_for_act(5)
            multiply(3)
            lo_norm(4)
            multiply(4)
            lo_norm(5)
            multiply(5)
            multiply(6)
            for k in range(7, K - 1):
                multiply(k)
                if k - 1 not in BY_POOL:
                    lo_prod(k - 1)
            lo_prod(K - 2)
            multiply(K - 1)
            lo_prod(K - 1)
            finish(QUARTERS - 1)

        @block.tensor
        def _(pe):
            def warm_up():
                pe.wait_ge(zero_ready, 1)
                for _ in range(WARM):
                    nc.tensor.matmul(outp[1][:, :], zero[:, 0:P], zero[:, :], start=True, stop=True)

            def turn_norm(g):
                if g == 0:
                    pe.wait_ge(ident_ready, 1)
                elif g == 2:
                    pe.wait_ge(nl_ready, 1)
                if g < BY_DVE:
                    pe.wait_ge(norm_ready, GROUPS[g].stop)
                else:
                    pe.wait_ge(norm_act_ready, GROUPS[g].stop - GROUPS[BY_DVE].start)
                for i in GROUPS[g]:
                    last = nc.tensor.transpose(turned_tile(g, i), xn[:, i, :], ident[:, :])
                last.then_inc(n_turned, 1)

            def turn_y(g):
                if g in OTHER_BANK:
                    pe.wait_ge(gbc_ready, STEPS)
                else:
                    pe.wait_ge(nl_ready, g)
                if g == BEHIND:
                    pe.wait_ge(acc_done, E)
                else:
                    pe.wait_ge(acc_last, CH)
                    if g > BEHIND + 1:
                        pe.wait_ge(acc_done, STEPS)
                for i in GROUPS[g]:
                    c = (i - TILES) * P
                    last = nc.tensor.transpose(turned_tile(g, i), acc[:, c:c + P], ident[:, :])
                last.then_inc(y_turned, 1)

            def gate(n):
                if n == 0:
                    pe.wait_ge(ones_ready, 1)
                    pe.wait_ge(nl_ready, 2)
                else:
                    pe.wait_ge(gbc_ready, n)
                if n == MASK_BY_POOL:
                    pe.wait_ge(mask_pool_ready, 1)
                else:
                    pe.wait_ge(mask_ready, n + 1 if n < MASK_BY_POOL else n)
                nc.tensor.matmul(gate_ps[:, :], ones[:, :], msk[:, n % MR, :],
                                 start=True, stop=True).then_inc(gate_done, 1)

            def by_hi(dst, wh, wl, xh, start=True):
                nc.tensor.matmul(dst, wh, xh, start=start, stop=False)
                nc.tensor.matmul(dst, wl, xh, start=False, stop=False)

            def by_lo(dst, wh, xl, stop=True):
                return nc.tensor.matmul(dst, wh, xl, start=False, stop=stop)

            def first_products_by_quarters():
                pe.wait_ge(w_lo, 1)
                for q in range(2):
                    pe.wait_ge(nh_ready, q + 1)
                    for m in range(CH):
                        w = slice(m * P, (m + 1) * P)
                        by_hi(quarter(hid[m], q), weh[:, 0, w], wel[:, 0, w], quarter(nh, q))
                        if m == 0:
                            pe.wait_ge(nl_ready, q + 1)
                        last = by_lo(quarter(hid[m], q), weh[:, 0, w], quarter(nl, q))
                        if q == 1:
                            last.then_inc(hid_done, 1)

            def first_product(m):
                n, c = m // CH, m % CH
                h, e = n // E, n % E
                if c == 0 and h == 0:
                    pe.wait_ge(w_lo, 2 * e + 1)
                if c == 0 and e == 0:
                    pe.wait_ge(nh_ready, BEHIND)
                if m >= HR:
                    pe.wait_ge(hl_ready, m - HR + 1)
                w = slice(c * P, (c + 1) * P)
                by_hi(hid[m % HR][:, :], weh[:, e, w], wel[:, e, w], half(nh, h))
                if c == 0 and e == 0:
                    pe.wait_ge(nl_ready, BEHIND)
                by_lo(hid[m % HR][:, :], weh[:, e, w], half(nl, h)).then_inc(hid_done, 1)

            def second_product(m):
                n, c = m // CH, m % CH
                e = n % E
                if c == 0 and n < E:
                    pe.wait_ge(w_lo, 2 * e + 2)
                if c == 0 and n >= 2:
                    pe.wait_ge(gated_ready, n - 1)
                pe.wait_ge(hh_ready, m + 1)
                w = slice((CH + c) * P, (CH + c + 1) * P)
                by_hi(outp[n % 2][:, :], weh[:, e, w], wel[:, e, w], hh[:, m % HR, :], start=(c == 0))
                pe.wait_ge(hl_ready, m + 1)
                by_lo(outp[n % 2][:, :], weh[:, e, w], hl[:, m % HR, :],
                      stop=(c == CH - 1)).then_inc(out_done, 1)

            def last_products_by_quarters():
                n = STEPS - 1
                pe.wait_ge(gated_ready, n - 1)
                for q in range(2):
                    dst = step_sum(n, slice(q * Q, (q + 1) * Q))
                    for m in range(n * CH, M):
                        c = m % CH
                        w = slice((CH + c) * P, (CH + c + 1) * P)
                        xh, xl = (quarter(t[:, m % HR, :], q) for t in (hh, hl))
                        if q == 0:
                            pe.wait_ge(hh_ready, m + 1)
                        by_hi(dst, weh[:, E - 1, w], wel[:, E - 1, w], xh, start=(c == 0))
                        if q == 0:
                            pe.wait_ge(hl_ready, m + 1)
                        last = by_lo(dst, weh[:, E - 1, w], xl, stop=(c == CH - 1))
                        if q == 0 and c == 0:
                            gate(n)
                    last.then_inc(out_done, 1)

            def gate_up(k):
                q, c = k // FC, k % FC
                if k == 0:
                    pe.wait_ge(w_lo, 2 * E + 3)
                if k < HR:
                    pe.wait_ge(hl_ready, M - HR + k + 1)
                    if k == SPARE:
                        pe.wait_ge(gated_ready, STEPS + 1)
                else:
                    pe.wait_ge(prod_ready, k - HR + 1)
                xh, xl = (quarter(t, QUARTERS + q) for t in (nh, nl))
                blocks = [(quarter(hid[k % HR], b), slice((b * FC + c) * P, (b * FC + c + 1) * P))
                          for b in range(2)]
                if c == 0:
                    pe.wait_ge(nh_ready, BEHIND + max(1, q))
                for b, (dst, w) in enumerate(blocks):
                    by_hi(dst, wfh[:, w], wfl[:, w], xh)
                    if c == 0 and b == 0:
                        pe.wait_ge(nl_ready, BEHIND + max(1, q))
                    last = by_lo(dst, wfh[:, w], xl)
                last.then_inc(up_done, 1)

            def down(k):
                q, c = k // FC, k % FC
                if c == 0:
                    if q == 0:
                        pe.wait_ge(gated_ready, STEPS - 1)
                    elif q == 1:
                        pe.wait_ge(gated_ready, STEPS + 1)
                    else:
                        pe.wait_ge(sum_scaled, q - 1)
                w = slice((2 * FC + c) * P, (2 * FC + c + 1) * P)
                dst = outp[q % 2][:, 0:Q]
                hi_taken(pe, k)
                by_hi(dst, wfh[:, w], wfl[:, w], fh[:, k, :], start=(c == 0))
                lo_taken(pe, k)
                by_lo(dst, wfh[:, w], fl[:, k, :], stop=(c == FC - 1)).then_inc(down_done, 1)

            warm_up()
            turn_norm(0)
            turn_norm(1)
            first_products_by_quarters()
            for m in range(CH, M + LAG - CH):
                if m == 14:
                    turn_norm(2)
                if m == 22:
                    turn_y(3)
                if m == 30:
                    turn_norm(3)
                if m < M:
                    first_product(m)
                if m >= LAG:
                    second_product(m - LAG)
                if m % CH and m > CH and m < M:
                    gate(m // CH - 1)
            last_products_by_quarters()
            gate_up(0)
            gate_up(1)
            turn_y(4)
            gate_up(2)
            turn_y(5)
            gate_up(3)
            gate_up(4)
            gate_up(5)
            down(0)
            turn_norm(4)
            down(1)
            gate_up(6)
            turn_norm(5)
            down(2)
            for k in range(7, K):
                gate_up(k)
                down(k - 4)
            for k in range(K - 4, K):
                down(k)


def kernel(x, ctx_512, itok_BxS2xS_0_7, L0_xattn_proj_in, L0_xattn_proj_out,
           L0_ffn_w_gate, L0_ffn_w_up, L0_ffn_w_down):
    import numpy as np
    import concourse.bacc as bacc
    from concourse import mybir
    from concourse.bass_utils import run_bass_kernel_spmd

    P = 128
    x = np.asarray(x)
    B, S, D = x.shape
    T = B * S
    win, wout = np.asarray(L0_xattn_proj_in), np.asarray(L0_xattn_proj_out)
    E, HID, _ = win.shape
    CH = HID // P
    rows = x.reshape(T, D)
    w_experts = np.concatenate(
        [win.transpose(2, 0, 1), wout.reshape(E, D, CH, P).transpose(3, 0, 2, 1).reshape(P, E, CH * D)], axis=2)
    down = np.asarray(L0_ffn_w_down).T
    w_ffn = np.concatenate(
        [np.asarray(L0_ffn_w_gate).T, np.asarray(L0_ffn_w_up).T,
         down.reshape(-1, P, D).transpose(1, 0, 2).reshape(P, -1)], axis=1)

    def choices_first(a):
        a = np.asarray(a).transpose(1, 0, 2).reshape(-1, T)
        return np.concatenate([a, a], axis=0)

    arrays = {
        "x_tok": rows.reshape(T // P, P, D).transpose(1, 0, 2),
        "x_feat": rows.T,
        "ctx_kt": choices_first(ctx_512),
        "ids_kt": choices_first(itok_BxS2xS_0_7),
        "w_experts": w_experts,
        "w_ffn": w_ffn,
    }
    arrays = {k: np.ascontiguousarray(v) for k, v in arrays.items()}
    nc = bacc.Bacc("TRN2", target_bir_lowering=False, num_devices=1)
    ins = [nc.dram_tensor(k, v.shape, mybir.dt.from_np(v.dtype), kind="ExternalInput").ap()
           for k, v in arrays.items()]
    out = nc.dram_tensor("out_feat", (D, T), mybir.dt.float32, kind="ExternalOutput").ap()
    xattn_ffn_program(nc, *ins, out)
    r = run_bass_kernel_spmd(nc, [arrays], core_ids=[0])
    return np.ascontiguousarray(r.results[0]["out_feat"].T).reshape(B, S, D)
```
